# Optimizing a Trainium2 kernel written in Bass

```python
import numpy as np
import jax
import jax.numpy as jnp

def _softmax(x, axis=-1):
    return jax.nn.softmax(x, axis=axis)

def _gelu(x):
    return jax.nn.gelu(x, approximate=True)

def _silu(x):
    return jax.nn.silu(x)

def _sigmoid(x):
    return jax.nn.sigmoid(x)

def _layernorm(x, axis=-1, eps=1e-05):
    m = jnp.mean(x, axis=axis, keepdims=True)
    v = jnp.var(x, axis=axis, keepdims=True)
    return (x - m) / jnp.sqrt(v + eps)

def _scatter_add(tgt, idx, src, axis=0):
    return tgt.at[idx].add(src)

def _segment_sum(src, seg, n):
    return jax.ops.segment_sum(src, seg, n)
kernel_name = 'mk_cond_resid_d2_seqx_r2_319e91'

def setup_inputs(seed: int=0):
    np.random.seed(seed)
    _w = jnp.asarray

    def _rec_inputs():
        import jax
        import jax.numpy as jnp
        _rk = jax.random.key(seed)
        x = -0.000125 + 0.9999 * jax.random.normal(jax.random.fold_in(_rk, 1), (8, 512, 2048), jnp.float32)
        _lenS = 512 - jax.random.randint(jax.random.fold_in(_rk, 7), (8,), 0, max(1, 512 // 4) + 1, jnp.int32)
        _lenS2 = 512 - jax.random.randint(jax.random.fold_in(_rk, 8), (8,), 0, max(1, 512 // 4) + 1, jnp.int32)
        itok_B_6_15 = jax.random.randint(jax.random.fold_in(_rk, 11), (8,), 6, 16, jnp.int32)
        itok_B_0_23 = jax.random.randint(jax.random.fold_in(_rk, 12), (8,), 0, 24, jnp.int32)
        return (x, itok_B_6_15, itok_B_0_23)
    x, itok_B_6_15, itok_B_0_23 = _rec_inputs()

    def _L0_cond_setup():
        import jax, jax.numpy as jnp
        import numpy as np
        B, S, D_IN, D_OUT = (4, 1024, 2048, 2048)
        RANK, MAX_LORAS = (16, 32)
        key = jax.random.key(seed)
        ks = jax.random.split(key, 6)
        x = jax.random.normal(ks[0], (B, S, D_IN), dtype=jnp.float32)
        adapter_ids = jax.random.randint(ks[1], (B,), 0, MAX_LORAS)
        base_weight = jax.random.normal(ks[2], (D_OUT, D_IN), dtype=jnp.float32) * D_IN ** (-0.5)
        base_bias = jax.random.normal(ks[3], (D_OUT,), dtype=jnp.float32) * 0.01
        lora_A_w = jax.random.normal(ks[4], (MAX_LORAS, RANK, D_IN), dtype=jnp.float32) * D_IN ** (-0.5)
        lora_B_w = jax.random.normal(ks[5], (MAX_LORAS, D_OUT, RANK), dtype=jnp.float32) * RANK ** (-0.5)
        return {'x': x, 'adapter_ids': adapter_ids, 'base_weight': base_weight, 'base_bias': base_bias, 'lora_A_w': lora_A_w, 'lora_B_w': lora_B_w}
    _L0_cond_all = _L0_cond_setup()
    _L0_cond_in = {k: v for k, v in _L0_cond_all.items() if k in ('base_weight', 'base_bias', 'lora_A_w', 'lora_B_w')}
    del _L0_cond_all

    def _L1_cond_setup():
        import jax, jax.numpy as jnp
        import numpy as np
        R = 16
        ALPHA = 32
        SCALING = ALPHA / R
        SLOTS = 32
        IN_F = 2048
        OUT_F = 2048
        B, T = (8, 512)
        key = jax.random.key(seed)
        k1, k2, k3, k4, k5, k6 = jax.random.split(key, 6)
        x = jax.random.normal(k1, (B, T, IN_F), dtype=jnp.float32)
        adapter_mapping = jax.random.randint(k2, (B,), 0, SLOTS, dtype=jnp.int32)
        W = jax.random.normal(k3, (OUT_F, IN_F), dtype=jnp.float32) * 0.02
        b = jax.random.normal(k4, (OUT_F,), dtype=jnp.float32) * 0.02
        lora_As = jax.random.normal(k5, (SLOTS, IN_F, R), dtype=jnp.float32) * 0.02
        lora_Bs = jax.random.normal(k6, (SLOTS, R, OUT_F), dtype=jnp.float32) * 0.02
        return {'x': x, 'adapter_mapping': adapter_mapping, 'W': W, 'b': b, 'lora_As': lora_As, 'lora_Bs': lora_Bs}
    _L1_cond_all = _L1_cond_setup()
    _L1_cond_in = {k: v for k, v in _L1_cond_all.items() if k in ('W', 'b', 'lora_As', 'lora_Bs')}
    del _L1_cond_all
    return {'x': x, 'itok_B_6_15': itok_B_6_15, 'itok_B_0_23': itok_B_0_23, 'L0_cond_base_weight': _L0_cond_in['base_weight'], 'L0_cond_base_bias': _L0_cond_in['base_bias'], 'L0_cond_lora_A_w': _L0_cond_in['lora_A_w'], 'L0_cond_lora_B_w': _L0_cond_in['lora_B_w'], 'L1_cond_W': _L1_cond_in['W'], 'L1_cond_b': _L1_cond_in['b'], 'L1_cond_lora_As': _L1_cond_in['lora_As'], 'L1_cond_lora_Bs': _L1_cond_in['lora_Bs']}

def reference(x, itok_B_6_15, itok_B_0_23, L0_cond_base_weight, L0_cond_base_bias, L0_cond_lora_A_w, L0_cond_lora_B_w, L1_cond_W, L1_cond_b, L1_cond_lora_As, L1_cond_lora_Bs):
    import jax
    import jax.numpy as jnp

    def _L0_cond_ref(x, adapter_ids, base_weight, base_bias, lora_A_w, lora_B_w):
        import jax, jax.numpy as jnp
        import numpy as np
        B, S, D_IN, D_OUT = (4, 1024, 2048, 2048)
        RANK, MAX_LORAS = (16, 32)
        result = jnp.einsum('bsd,od->bso', x, base_weight) + base_bias
        A = lora_A_w[adapter_ids]
        Bw = lora_B_w[adapter_ids]
        h = jnp.einsum('bsd,brd->bsr', x, A)
        lora_out = jnp.einsum('bsr,bor->bso', h, Bw)
        result = result + lora_out
        return result.astype(x.dtype)

    def _L1_cond_ref(x, adapter_mapping, W, b, lora_As, lora_Bs):
        import jax, jax.numpy as jnp
        import numpy as np
        R = 16
        ALPHA = 32
        SCALING = ALPHA / R
        SLOTS = 32
        IN_F = 2048
        OUT_F = 2048
        B, T = (8, 512)
        base_out = jnp.einsum('bti,oi->bto', x, W) + b
        A = lora_As[adapter_mapping]
        Bm = lora_Bs[adapter_mapping]
        lora_h = jnp.einsum('bti,bir->btr', x, A)
        lora_out = jnp.einsum('btr,bro->bto', lora_h, Bm)
        return base_out + lora_out * SCALING
    x = x + _L0_cond_ref(x, itok_B_6_15, L0_cond_base_weight, L0_cond_base_bias, L0_cond_lora_A_w, L0_cond_lora_B_w)
    x = x + _L1_cond_ref(x, itok_B_0_23, L1_cond_W, L1_cond_b, L1_cond_lora_As, L1_cond_lora_Bs)
    return x

_drawn_inputs = setup_inputs


def setup_inputs(seed=0):
    import zlib

    import numpy as np

    out = dict(_drawn_inputs(seed))
    spreads = {}
    factors = {'L0_cond_base_bias': 8.0, 'L1_cond_b': 7.966}
    for name, (base, spread) in spreads.items():
        noise = np.random.default_rng([zlib.crc32(name.encode()), seed]).standard_normal(out[name].shape)
        drawn = base * np.exp(spread * noise) if base else spread * noise
        out[name] = jnp.asarray(drawn.astype(out[name].dtype))
    for name, factor in factors.items():
        out[name] = (out[name] * factor).astype(out[name].dtype)
    return out
```

```python
import concourse.bass as bass
from concourse import mybir
from contextlib import ExitStack

P = 128


def two_layer_lora_kernel(nc, x_t, ids0, ids1, w0_t, w1_t, bias0, bias1,
                          lora_a0, lora_a1, lora_b0, lora_b1, out_t):
    fp32, f32r, i32 = mybir.dt.float32, mybir.dt.float32r, mybir.dt.int32
    ALU = mybir.AluOpType
    ACT = mybir.ActivationFunctionType

    BATCH, KT, _, T = x_t.shape
    MT = w0_t.shape[0]
    SLOTS, RANK, _ = lora_b0.shape
    PAIRS = MT // 2
    HALVES = 2
    KH = KT // HALVES
    HW = KH * P
    REP = P // RANK
    SCALE = (1.0, 2.0)
    QUADS = P // 32
    LAG = 4
    XR = 4
    w_t, bias_d = (w0_t, w1_t), (bias0, bias1)
    lora_a, lora_b, ids_d = (lora_a0, lora_a1), (lora_b0, lora_b1), (ids0, ids1)
    assert KT == MT and MT % 2 == 0 and REP * RANK == P and 2 * RANK == 32

    ctx = ExitStack()
    with ctx:
        def sb(name, shape, dt=fp32):
            return ctx.enter_context(nc.sbuf_tensor(name, shape, dt))

        def pb(name):
            return ctx.enter_context(nc.psum_tensor(name, [P, T], fp32))

        def sem(name):
            return ctx.enter_context(nc.semaphore(name))

        act_hi = [sb(f"act_hi{i}", [P, KT, T], f32r) for i in range(2)]
        act_lo = [sb(f"act_lo{i}", [P, KT, T], f32r) for i in range(2)]
        x_raw = sb("x_raw", [P, XR, T])
        w_raw = sb("w_raw", [P, 2, HALVES, HW])
        w_hi = sb("w_hi", [P, 2, KT, P], f32r)
        w_lo = sb("w_lo", [P, 2, KT, P], f32r)
        a_raw = sb("a_raw", [P, 2, KT, RANK])
        a_split = sb("a_split", [P, KT, QUADS, 2 * RANK], f32r)
        b_raw = sb("b_raw", [P, 2, P])
        b_split = sb("b_split", [P, 2, P], f32r)
        h_split = sb("h_split", [P, T], f32r)
        bias = sb("bias", [P, 2, MT])
        ids = sb("ids", [1, 2, BATCH], i32)
        resid = sb("resid", [P, T])
        y_tile = sb("y_tile", [P, 2, T])

        acc = [pb("acc_even"), pb("acc_odd")]
        h_acc = pb("h_acc")

        ids_loaded = sem("ids_loaded")
        bias_loaded = sem("bias_loaded")
        w_loaded = [[sem(f"w_loaded{i}{h}") for h in range(HALVES)] for i in range(2)]
        x0_loaded = [sem(f"x0_loaded{i}") for i in range(XR)]
        x_loaded = [sem(f"x_loaded{i}") for i in range(2)]
        a_loaded = [sem(f"a_loaded{i}") for i in range(2)]
        b_loaded = [sem(f"b_loaded{i}") for i in range(2)]
        out_stored = [sem(f"out_stored{i}") for i in range(2)]
        w_hi_ready = sem("w_hi_ready")
        w_lo_ready = sem("w_lo_ready")
        x_hi_ready = sem("x_hi_ready")
        x_lo_ready = sem("x_lo_ready")
        y_hi_ready = sem("y_hi_ready")
        y_lo_ready = sem("y_lo_ready")
        a_hi_ready = sem("a_hi_ready")
        a_lo_ready = sem("a_lo_ready")
        b_hi_ready = sem("b_hi_ready")
        b_lo_ready = sem("b_lo_ready")
        h_done = sem("h_done")
        h_hi_ready = sem("h_hi_ready")
        h_lo_ready = sem("h_lo_ready")
        resid_ready = sem("resid_ready")
        main_done = [sem(f"main_done{i}") for i in range(2)]
        acc_done = [sem(f"acc_done{i}") for i in range(2)]
        acc_read = [sem(f"acc_read{i}") for i in range(2)]

        block = ctx.enter_context(nc.Block())

        def layer_no(b, l):
            return b * 2 + l

        def pair_no(b, l, j):
            return b * (2 * PAIRS) + l * PAIRS + j

        def load_b(eng, adapter, l, m, i):
            rows = lora_b[l][bass.ds(adapter, 1), :, bass.ds(m * P, P)].broadcast_to([REP, RANK, P])
            eng.dma_start(b_raw[:, i, :], rows).then_inc(b_loaded[i], 16)

        def load_a(eng, adapter, l):
            eng.dma_start(a_raw[:, l, :, :],
                          lora_a[l][bass.ds(adapter, 1), :, :]
                          .rearrange("o p (k r) -> (o p) k r", r=RANK)).then_inc(a_loaded[l], 16)

        def adapter_of(eng, b, l):
            return eng.value_load(ids[0:1, l, bass.ds(b, 1)], min_val=0, max_val=SLOTS - 1)

        def a_copies(l):
            return a_raw[:, l, :, :].rearrange("p k (o r) -> p k o r", o=1).broadcast_to([P, KT, QUADS, RANK])

        @block.sync
        def _(sp):
            def load_pair(adapter, b, l, j, q, wait):
                for i in range(2):
                    for h in range(HALVES):
                        if wait:
                            sp.wait_ge(w_lo_ready, (q - 1) * 4 + i * 2 + h + 1)
                        sp.dma_start(w_raw[:, i, h, :],
                                     w_t[l][bass.ds(j * 2 + i, 1), :, h * HW:(h + 1) * HW]
                                     .rearrange("o p n -> (o p) n")).then_inc(w_loaded[i][h], 16)
                    if wait:
                        sp.wait_ge(b_lo_ready, (q - 1) * 2 + i + 1)
                    load_b(sp, adapter, l, j * 2 + i, i)

            for k in range(KT):
                if k % KH == 0:
                    h = k // KH
                    sp.dma_start(w_raw[:, 0, h, :], w_t[0][0, :, h * HW:(h + 1) * HW]).then_inc(w_loaded[0][h], 16)
                if k >= XR:
                    sp.wait_ge(x_lo_ready, k - XR + 1)
                sp.dma_start(x_raw[:, k % XR, :], x_t[0, k, :, :]).then_inc(x0_loaded[k % XR], 16)
                if k >= KT - HALVES:
                    h = k - (KT - HALVES)
                    sp.dma_start(w_raw[:, 1, h, :], w_t[0][1, :, h * HW:(h + 1) * HW]).then_inc(w_loaded[1][h], 16)
            sp.wait_ge(ids_loaded, 32)

            def batch(b, last):
                this0 = adapter_of(sp, b, 0)
                this1 = adapter_of(sp, b, 1)
                load_a(sp, this1, 1)
                with sp.Fori(1, PAIRS) as j:
                    load_pair(this0, b, 0, j, pair_no(b, 0, j), True)
                load_pair(this1, b, 1, 0, pair_no(b, 1, 0), True)
                if not last:
                    after0 = adapter_of(sp, b + 1, 0)
                    sp.wait_ge(a_lo_ready, layer_no(b, 1))
                    load_a(sp, after0, 0)

                def load_x(j):
                    for i in range(2):
                        sp.wait_ge(x_lo_ready, b * KT + KT + j * 2 + i - 1)
                        sp.dma_start(x_raw[:, i, :],
                                     x_t[bass.ds(b + 1, 1), bass.ds(j * 2 + i, 1), :, :]
                                     .rearrange("a c p t -> (a c p) t")).then_inc(x_loaded[i], 16)

                if not last:
                    load_x(0)
                with sp.Fori(1, PAIRS) as j:
                    load_pair(this1, b, 1, j, pair_no(b, 1, j), True)
                    if not last:
                        load_x(j)
                if not last:
                    load_pair(after0, b + 1, 0, 0, pair_no(b, 2, 0), True)

            with sp.Fori(0, BATCH - 1) as b:
                batch(b, False)
            batch(BATCH - 1, True)

        @block.scalar
        def _(act):
            for i in range(2):
                act.sem_inc(out_stored[i], 16)
            for l in range(2):
                act.dma_start(ids[0:1, l, :], ids_d[l].rearrange("(o n) -> o n", o=1)).then_inc(ids_loaded, 16)

            def w_split_hi(q, i, halves=range(HALVES)):
                for h in halves:
                    act.wait_ge(w_loaded[i][h], q * 16 + 16)
                    nc.scalar.activation(
                        w_hi[:, i, h * KH:(h + 1) * KH, :].rearrange("p k n -> p (k n)"),
                        w_raw[:, i, h, :], ACT.Copy).then_inc(w_hi_ready, 1)

            def b_split_hi(q, i):
                act.wait_ge(b_loaded[i], q * 16 + 16)
                nc.scalar.activation(b_split[:, i, :], b_raw[:, i, :], ACT.Copy).then_inc(b_hi_ready, 1)

            def a_hi(b, l):
                act.wait_ge(a_loaded[l], b * 16 + 16)
                nc.scalar.activation(a_split[:, :, :, 0:RANK], a_copies(l), ACT.Copy).then_inc(a_hi_ready, 1)

            for k in range(KT):
                if k % KH == 0:
                    w_split_hi(0, 0, [k // KH])
                act.wait_ge(x0_loaded[k % XR], (k // XR + 1) * 16)
                nc.scalar.activation(act_hi[0][:, k, :], x_raw[:, k % XR, :], ACT.Copy).then_inc(x_hi_ready, 1)
                if k == 1:
                    act.wait_ge(ids_loaded, 32)
                    first = adapter_of(act, 0, 0)
                    load_a(act, first, 0)
                    for i in range(2):
                        load_b(act, first, 0, i, i)
                    for l in range(2):
                        act.dma_start(bias[:, l, :], bias_d[l]).then_inc(bias_loaded, 16)
                if k == LAG:
                    a_hi(0, 0)
            w_split_hi(0, 1)
            for i in range(2):
                b_split_hi(0, i)

            def h_hi(b, l):
                act.wait_ge(h_done, layer_no(b, l) + 1)
                nc.scalar.activation(h_split[:, :], h_acc[:, :], ACT.Copy,
                                     scale=SCALE[l]).then_inc(h_hi_ready, 1)

            def tile(b, l, j, i, first, last, end):
                q = pair_no(b, l, j)
                if not end:
                    act.wait_ge(main_done[i], q + 1)
                    w_split_hi(q + 1, i)
                if first and i == 0:
                    h_hi(b, l)
                act.wait_ge(acc_read[i], q + 2)
                if not end:
                    b_split_hi(q + 1, i)
                if l == 0:
                    nc.scalar.activation(act_hi[1][:, bass.ds(j * 2 + i, 1), :].rearrange("p k t -> p (k t)"),
                                         y_tile[:, i, :], ACT.Copy).then_inc(y_hi_ready, 1)
                else:
                    act.dma_start(out_t[bass.ds(b, 1), bass.ds(j * 2 + i, 1), :, :]
                                  .rearrange("a c p t -> (a c p) t"), y_tile[:, i, :]).then_inc(out_stored[i], 16)
                if l == 1 and not last:
                    act.wait_ge(acc_read[1], pair_no(b, 1, 0) + 1)
                    act.wait_ge(x_loaded[i], b * (16 * PAIRS) + j * 16 + 16)
                    nc.scalar.activation(act_hi[0][:, bass.ds(j * 2 + i, 1), :].rearrange("p k t -> p (k t)"),
                                         x_raw[:, i, :], ACT.Copy).then_inc(x_hi_ready, 1)

            def batch(b, last):
                for l in range(2):
                    for i in range(2):
                        tile(b, l, 0, i, True, last, False)
                    ends = last and l == 1
                    if not ends:
                        a_hi(b + l, 1 - l)
                    with act.Fori(1, PAIRS - ends) as j:
                        for i in range(2):
                            tile(b, l, j, i, False, last, False)
                    if ends:
                        for i in range(2):
                            tile(b, l, PAIRS - 1, i, False, last, True)

            with act.Fori(0, BATCH - 1) as b:
                batch(b, False)
            batch(BATCH - 1, True)
            for i in range(2):
                act.wait_ge(out_stored[i], 16 + 16 * BATCH * PAIRS)

        @block.vector
        def _(dve):
            def f(ap):
                return ap.bitcast(fp32)

            def flat(ap):
                return ap.rearrange("p k n -> p (k n)")

            for i in range(2):
                dve.sem_inc(acc_read[i], 1)

            def w_split_lo(q, i, halves=range(HALVES)):
                for h in halves:
                    dve.wait_ge(w_hi_ready, q * 4 + i * 2 + h + 1)
                    ks = slice(h * KH, (h + 1) * KH)
                    nc.vector.tensor_tensor(flat(w_lo[:, i, ks, :]), w_raw[:, i, h, :],
                                            f(flat(w_hi[:, i, ks, :])), ALU.subtract).then_inc(w_lo_ready, 1)

            def b_split_lo(q, i):
                dve.wait_ge(b_hi_ready, q * 2 + i + 1)
                half = slice(P // 2, P)
                nc.vector.tensor_tensor(b_split[half, i, :], b_raw[half, i, :],
                                        f(b_split[half, i, :]), ALU.subtract).then_inc(b_lo_ready, 1)

            def a_lo(b, l):
                dve.wait_ge(a_hi_ready, layer_no(b, l) + 1)
                nc.vector.tensor_tensor(a_split[:, :, :, RANK:2 * RANK], a_copies(l),
                                        f(a_split[:, :, :, 0:RANK]), ALU.subtract).then_inc(a_lo_ready, 1)

            for k in range(KT):
                if k % KH == 0:
                    w_split_lo(0, 0, [k // KH])
                dve.wait_ge(x_hi_ready, k + 1)
                nc.vector.tensor_tensor(act_lo[0][:, k, :], x_raw[:, k % XR, :], f(act_hi[0][:, k, :]),
                                        ALU.subtract).then_inc(x_lo_ready, 1)
                if k == LAG:
                    a_lo(0, 0)
            w_split_lo(0, 1)
            for i in range(2):
                b_split_lo(0, i)
            dve.wait_ge(bias_loaded, 32)

            def h_lo(b, l):
                dve.wait_ge(h_hi_ready, layer_no(b, l) + 1)
                for quad in (1, 3):
                    rows = slice(quad * 32, quad * 32 + 32)
                    last = nc.vector.scalar_tensor_tensor(h_split[rows, :], h_acc[rows, :], SCALE[l],
                                                          f(h_split[rows, :]), ALU.mult, ALU.subtract)
                last.then_inc(h_lo_ready, 1)

            def tile(b, l, j, i, first, last, end):
                q = pair_no(b, l, j)
                m = bass.ds(j * 2 + i, 1)
                dve.wait_ge(y_lo_ready if l else x_lo_ready, b * KT + j * 2 + i + 1)
                dve.wait_ge(acc_read[1 - i], q + i + 1)
                nc.vector.tensor_tensor(resid[:, :], flat(f(act_hi[l][:, m, :])), flat(f(act_lo[l][:, m, :])),
                                        ALU.add).then_inc(resid_ready, 1)
                if not end:
                    w_split_lo(q + 1, i)
                if first and i == 0:
                    h_lo(b, l)
                dve.wait_ge(resid_ready, q * 2 + i + 1)
                dve.wait_ge(acc_done[i], q + 1)
                dve.wait_ge(out_stored[i], b * (16 * PAIRS) + (j * 16 if l else 0) + 16)
                nc.vector.scalar_tensor_tensor(y_tile[:, i, :], acc[i][:, :], bias[:, l, m], resid[:, :],
                                               ALU.add, ALU.add).then_inc(acc_read[i], 1)
                if not end:
                    b_split_lo(q + 1, i)
                if l == 0:
                    dve.wait_ge(y_hi_ready, b * MT + j * 2 + i + 1)
                    nc.vector.tensor_tensor(flat(act_lo[1][:, m, :]), y_tile[:, i, :], flat(f(act_hi[1][:, m, :])),
                                            ALU.subtract).then_inc(y_lo_ready, 1)
                elif not last:
                    dve.wait_ge(x_hi_ready, b * KT + KT + j * 2 + i + 1)
                    nc.vector.tensor_tensor(flat(act_lo[0][:, m, :]), x_raw[:, i, :], flat(f(act_hi[0][:, m, :])),
                                            ALU.subtract).then_inc(x_lo_ready, 1)

            def batch(b, last):
                for l in range(2):
                    for i in range(2):
                        tile(b, l, 0, i, True, last, False)
                    ends = last and l == 1
                    if not ends:
                        a_lo(b + l, 1 - l)
                    with dve.Fori(1, PAIRS - ends) as j:
                        for i in range(2):
                            tile(b, l, j, i, False, last, False)
                    if ends:
                        for i in range(2):
                            tile(b, l, PAIRS - 1, i, False, last, True)

            with dve.Fori(0, BATCH - 1) as b:
                batch(b, False)
            batch(BATCH - 1, True)

        @block.tensor
        def _(pe):
            def main(b, l, j, i, first, ks):
                q = pair_no(b, l, j)
                for k in ks:
                    if k == 0:
                        pe.wait_ge(acc_read[i], q + 1)
                    if k % KH == 0:
                        pe.wait_ge(w_lo_ready, q * 4 + i * 2 + k // KH + 1)
                    if first and i == 0:
                        pe.wait_ge(y_lo_ready if l else x_lo_ready, b * KT + k + 1)
                    nc.tensor.matmul(acc[i][:, :], w_hi[:, i, k, :], act_hi[l][:, k, :],
                                     start=(k == 0), stop=False)
                    nc.tensor.matmul(acc[i][:, :], w_hi[:, i, k, :], act_lo[l][:, k, :],
                                     start=False, stop=False)
                    mm = nc.tensor.matmul(acc[i][:, :], w_lo[:, i, k, :], act_hi[l][:, k, :],
                                          start=False, stop=False)
                    if k == KT - 1:
                        mm.then_inc(main_done[i], 1)

            def down(b, l, k):
                if k == 0:
                    pe.wait_ge(a_lo_ready, layer_no(b, l) + 1)
                cols = a_split[:, k, :, :].rearrange("p c n -> p (c n)")
                nc.tensor.matmul(h_acc[:, :], cols, act_hi[l][:, k, :], start=(k == 0), stop=False)
                mm = nc.tensor.matmul(h_acc[:, :], cols, act_lo[l][:, k, :],
                                      start=False, stop=(k == KT - 1))
                if k == KT - 1:
                    mm.then_inc(h_done, 1)

            def up(b, l, j, i):
                pe.wait_ge(b_lo_ready, pair_no(b, l, j) * 2 + i + 1)
                nc.tensor.matmul(acc[i][:, :], b_split[:, i, :], h_split[:, :],
                                 start=False, stop=True).then_inc(acc_done[i], 1)

            with pe.Fori(0, BATCH) as b:
                for l in range(2):
                    for k in range(KT + LAG):
                        if k < KT:
                            main(b, l, 0, 0, True, [k])
                        if k >= LAG:
                            down(b, l, k - LAG)
                    main(b, l, 0, 1, True, range(KH))
                    pe.wait_ge(h_lo_ready, layer_no(b, l) + 1)
                    up(b, l, 0, 0)
                    main(b, l, 0, 1, True, range(KH, KT))
                    up(b, l, 0, 1)
                    with pe.Fori(1, PAIRS) as j:
                        for i in range(2):
                            main(b, l, j, i, False, range(KT))
                            up(b, l, j, i)


def kernel(x, itok_B_6_15, itok_B_0_23, L0_cond_base_weight, L0_cond_base_bias, L0_cond_lora_A_w,
           L0_cond_lora_B_w, L1_cond_W, L1_cond_b, L1_cond_lora_As, L1_cond_lora_Bs):
    import numpy as np
    import concourse.bacc as bacc
    from concourse.bass_utils import run_bass_kernel_spmd

    batch, tokens, dim = x.shape
    tiles = dim // P
    slots, rank, _ = L0_cond_lora_A_w.shape

    def w_tiles(w):
        w = np.asarray(w).reshape(tiles, P, tiles, P)
        return w.transpose(0, 3, 2, 1).reshape(tiles, P, dim)

    def columns(v):
        return np.asarray(v).reshape(tiles, P).T

    arrays = {
        "x_t": np.asarray(x).reshape(batch, tokens, tiles, P).transpose(0, 2, 3, 1),
        "ids0": np.asarray(itok_B_6_15),
        "ids1": np.asarray(itok_B_0_23),
        "w0_t": w_tiles(L0_cond_base_weight),
        "w1_t": w_tiles(L1_cond_W),
        "bias0": columns(L0_cond_base_bias),
        "bias1": columns(L1_cond_b),
        "lora_a0": np.asarray(L0_cond_lora_A_w).reshape(slots, rank, tiles, P).transpose(0, 3, 2, 1)
                     .reshape(slots, P, tiles * rank),
        "lora_a1": np.asarray(L1_cond_lora_As).reshape(slots, tiles, P, rank).transpose(0, 2, 1, 3)
                     .reshape(slots, P, tiles * rank),
        "lora_b0": np.asarray(L0_cond_lora_B_w).transpose(0, 2, 1),
        "lora_b1": np.asarray(L1_cond_lora_Bs),
    }
    arrays = {name: np.ascontiguousarray(a) for name, a in arrays.items()}
    nc = bacc.Bacc("TRN2", target_bir_lowering=False, num_devices=1)
    args = [nc.dram_tensor(name, a.shape, mybir.dt.from_np(a.dtype), kind="ExternalInput").ap()
            for name, a in arrays.items()]
    out = nc.dram_tensor("out_t", (batch, tiles, P, tokens), mybir.dt.float32, kind="ExternalOutput").ap()
    two_layer_lora_kernel(nc, *args, out)
    r = run_bass_kernel_spmd(nc, [arrays], core_ids=[0])
    got = r.results[0]["out_t"]
    return np.ascontiguousarray(got.transpose(0, 3, 1, 2).reshape(batch, tokens, dim))
```
